# Optimizing a Trainium2 kernel written in Bass

```python
import numpy as np
import jax
import jax.numpy as jnp

def _softmax(x, axis=-1):
    return jax.nn.softmax(x, axis=axis)

def _gelu(x):
    return jax.nn.gelu(x, approximate=True)

def _silu(x):
    return jax.nn.silu(x)

def _sigmoid(x):
    return jax.nn.sigmoid(x)

def _layernorm(x, axis=-1, eps=1e-05):
    m = jnp.mean(x, axis=axis, keepdims=True)
    v = jnp.var(x, axis=axis, keepdims=True)
    return (x - m) / jnp.sqrt(v + eps)

def _scatter_add(tgt, idx, src, axis=0):
    return tgt.at[idx].add(src)

def _segment_sum(src, seg, n):
    return jax.ops.segment_sum(src, seg, n)
kernel_name = 'mk_rec_standalone_d1_rec_r8_47feda'

def setup_inputs(seed: int=0):
    np.random.seed(seed)
    _w = jnp.asarray

    def _rec_inputs():
        import jax
        import jax.numpy as jnp
        _rk = jax.random.key(seed)
        r_x = jax.random.bernoulli(jax.random.fold_in(_rk, 1), 0.0003262, (512, 12288)).astype(jnp.float32)
        return r_x
    r_x = _rec_inputs()

    def _L0_rec_setup():
        import jax, jax.numpy as jnp
        import numpy as np
        B = 256
        IN_DIM = 12288
        H1 = 256
        H2 = 32
        key = jax.random.key(seed)
        ks = jax.random.split(key, 7)
        x = (jax.random.uniform(ks[0], (B, IN_DIM), dtype=jnp.float32) < 32.0 / IN_DIM).astype(jnp.float32)
        s1 = 1.0 / np.sqrt(IN_DIM)
        s2 = 1.0 / np.sqrt(H1)
        s3 = 1.0 / np.sqrt(H2)
        return {'x': x, 'W1': jax.random.normal(ks[1], (H1, IN_DIM), dtype=jnp.float32) * s1, 'b1': jax.random.normal(ks[2], (H1,), dtype=jnp.float32) * s1, 'W2': jax.random.normal(ks[3], (H2, H1), dtype=jnp.float32) * s2, 'b2': jax.random.normal(ks[4], (H2,), dtype=jnp.float32) * s2, 'Wout': jax.random.normal(ks[5], (1, H2), dtype=jnp.float32) * s3, 'bout': jax.random.normal(ks[6], (1,), dtype=jnp.float32) * s3}
    _L0_rec_all = _L0_rec_setup()
    _L0_rec_in = {k: v for k, v in _L0_rec_all.items() if k in ('W1', 'b1', 'W2', 'b2', 'Wout', 'bout')}
    del _L0_rec_all
    return {'r_x': r_x, 'L0_rec_W1': _L0_rec_in['W1'], 'L0_rec_b1': _L0_rec_in['b1'], 'L0_rec_W2': _L0_rec_in['W2'], 'L0_rec_b2': _L0_rec_in['b2'], 'L0_rec_Wout': _L0_rec_in['Wout'], 'L0_rec_bout': _L0_rec_in['bout']}

def reference(r_x, L0_rec_W1, L0_rec_b1, L0_rec_W2, L0_rec_b2, L0_rec_Wout, L0_rec_bout):
    import jax
    import jax.numpy as jnp

    def _L0_rec_ref(x, W1, b1, W2, b2, Wout, bout):
        import jax, jax.numpy as jnp
        import numpy as np
        B = 256
        IN_DIM = 12288
        H1 = 256
        H2 = 32
        h1 = jax.nn.relu(jnp.dot(x, W1.T) + b1)
        h2 = jax.nn.relu(jnp.dot(h1, W2.T) + b2)
        out = jnp.dot(h2, Wout.T) + bout
        return out
    y = _L0_rec_ref(r_x, L0_rec_W1, L0_rec_b1, L0_rec_W2, L0_rec_b2, L0_rec_Wout, L0_rec_bout)
    return y

_drawn_inputs = setup_inputs


def setup_inputs(seed=0):
    import zlib

    import numpy as np

    out = dict(_drawn_inputs(seed))
    spreads = {}
    factors = {'L0_rec_b1': 4.287}
    for name, (base, spread) in spreads.items():
        noise = np.random.default_rng([zlib.crc32(name.encode()), seed]).standard_normal(out[name].shape)
        drawn = base * np.exp(spread * noise) if base else spread * noise
        out[name] = jnp.asarray(drawn.astype(out[name].dtype))
    for name, factor in factors.items():
        out[name] = (out[name] * factor).astype(out[name].dtype)
    return out
```

```python
from contextlib import ExitStack

import concourse.bass as bass
from concourse import mybir

P = 128
NB = 512
T = 4
RING = 4

F32 = mybir.dt.float32
ACT = mybir.ActivationFunctionType
ALU = mybir.AluOpType


def bass_three_layer_mlp(nc: bass.Bass, x, w1, b1, w2, b2, wout, bout, out):
    chunks = x.shape[0]
    h1_halves = w1.shape[2] // T // P
    h2_dim = w2.shape[2]
    H1 = h1_halves * P
    rounds = chunks // RING

    with ExitStack() as ctx:
        def sb(name, shape, dt=F32):
            return ctx.enter_context(nc.sbuf_tensor(name, shape, dt))

        def psum(name, shape):
            return ctx.enter_context(nc.psum_tensor(name, shape, F32))

        def sem(name):
            return ctx.enter_context(nc.semaphore(name))

        x_raw = sb("x_raw", [P, RING, T * NB])
        w_raw = sb("w_raw", [P, RING, T * H1])
        zeros = sb("zeros", [P, NB])
        b1_sb = sb("b1_sb", [P, h1_halves])
        w2_sb = sb("w2_sb", [P, h1_halves, h2_dim])
        b2_sb = sb("b2_sb", [h2_dim, 1])
        wout_sb = sb("wout_sb", [h2_dim, 1])
        bout_sb = sb("bout_sb", [1, 1])
        h1 = sb("h1", [P, h1_halves, NB])
        h2 = sb("h2", [h2_dim, NB])
        y = sb("y", [1, NB])

        h1_ps = psum("h1_ps", [P, h1_halves, NB])
        h2_ps = psum("h2_ps", [h2_dim, NB])
        y_ps = psum("y_ps", [1, NB])

        x_landed = [sem(f"x_landed{s}") for s in range(RING)]
        w_landed = [sem(f"w_landed{s}") for s in range(RING)]
        small_landed = sem("small_landed")
        zeros_set = sem("zeros_set")
        chunk_used = sem("chunk_used")
        h1_summed = sem("h1_summed")
        h1_ready = sem("h1_ready")
        h2_summed = sem("h2_summed")
        h2_ready = sem("h2_ready")
        y_summed = sem("y_summed")
        y_ready = sem("y_ready")
        out_stored = sem("out_stored")

        block = ctx.enter_context(nc.Block())

        @block.sync
        def _(sp):
            def load(c, s):
                sp.dma_start(w_raw[:, s, :], w1[c]).then_inc(w_landed[s], 16)
                sp.dma_start(x_raw[:, s, :], x[c]).then_inc(x_landed[s], 16)

            for s in range(RING):
                load(s, s)
            for dst, src in ((b1_sb, b1), (w2_sb, w2), (b2_sb, b2), (wout_sb, wout), (bout_sb, bout)):
                sp.dma_start(dst[:], src).then_inc(small_landed, 16)
            with sp.Fori(1, rounds) as r:
                for s in range(RING):
                    sp.wait_ge(chunk_used, (r - 1) * RING + s + 1)
                    load(r * RING + s, s)
            sp.wait_ge(y_ready, 1)
            sp.dma_start(out, y[:]).then_inc(out_stored, 16)
            sp.wait_ge(out_stored, 16)

        @block.tensor
        def _(pe):
            pe.wait_ge(zeros_set, 1)
            for m in range(h1_halves):
                nc.tensor.matmul(h1_ps[:, m, :], zeros[:, 0:P], zeros[:], start=True, stop=False)
            with pe.Fori(0, rounds) as r:
                for s in range(RING):
                    pe.wait_ge(w_landed[s], (r + 1) * 16)
                    pe.wait_ge(x_landed[s], (r + 1) * 16)
                    for t in range(T):
                        for m in range(h1_halves):
                            last = nc.tensor.matmul(
                                h1_ps[:, m, :], w_raw[:, s, t * H1 + m * P:t * H1 + (m + 1) * P],
                                x_raw[:, s, t * NB:(t + 1) * NB], start=False, stop=False)
                    last.then_inc(chunk_used, 1)
            for m in range(h1_halves):
                nc.tensor.matmul(h1_ps[:, m, :], zeros[:, 0:P], zeros[:], start=False, stop=True).then_inc(h1_summed, 1)
            pe.wait_ge(small_landed, 16 * 5)
            for m in range(h1_halves):
                pe.wait_ge(h1_ready, m + 1)
                last = nc.tensor.matmul(h2_ps[:], w2_sb[:, m, :], h1[:, m, :],
                                        start=(m == 0), stop=(m == h1_halves - 1))
            last.then_inc(h2_summed, 1)
            pe.wait_ge(h2_ready, 1)
            nc.tensor.matmul(y_ps[:], wout_sb[:], h2[:], start=True, stop=True).then_inc(y_summed, 1)

        @block.vector
        def _(dve):
            nc.vector.memset(zeros[:], 0.0).then_inc(zeros_set, 1)

        @block.scalar
        def _(act):
            act.wait_ge(small_landed, 16 * 5)
            for m in range(h1_halves):
                act.wait_ge(h1_summed, m + 1)
                nc.scalar.activation(h1[:, m, :], h1_ps[:, m, :], ACT.Relu,
                                     bias=b1_sb[:, m:m + 1]).then_inc(h1_ready, 1)
            act.wait_ge(h2_summed, 1)
            nc.scalar.activation(h2[:], h2_ps[:], ACT.Relu, bias=b2_sb[:]).then_inc(h2_ready, 1)
            act.wait_ge(y_summed, 1)
            nc.scalar.activation(y[:], y_ps[:], ACT.Identity, bias=bout_sb[:]).then_inc(y_ready, 1)


def kernel(r_x, L0_rec_W1, L0_rec_b1, L0_rec_W2, L0_rec_b2, L0_rec_Wout, L0_rec_bout):
    import numpy as np
    import concourse.bacc as bacc
    from concourse.bass_utils import run_bass_kernel_spmd as run

    def chunked(a):
        rows, K = a.shape
        return np.ascontiguousarray(a.reshape(rows, K // (P * T), P, T).transpose(1, 2, 3, 0)).reshape(
            K // (P * T), P, T * rows)

    def halves(a):
        rows, H1 = a.shape
        return np.ascontiguousarray(a.reshape(rows, H1 // P, P).transpose(2, 1, 0))

    r_x, W1, b1, W2, b2, Wout, bout = (
        np.asarray(a) for a in (r_x, L0_rec_W1, L0_rec_b1, L0_rec_W2, L0_rec_b2, L0_rec_Wout, L0_rec_bout))
    arrays = {
        "x": chunked(r_x),
        "w1": chunked(W1),
        "b1": np.ascontiguousarray(b1.reshape(-1, P).T),
        "w2": halves(W2),
        "b2": b2.reshape(-1, 1),
        "wout": np.ascontiguousarray(Wout.T),
        "bout": bout.reshape(1, 1),
    }
    nc = bacc.Bacc("TRN2", target_bir_lowering=False, num_devices=1)
    args = [nc.dram_tensor(n, a.shape, mybir.dt.from_np(a.dtype), kind="ExternalInput").ap() for n, a in arrays.items()]
    out = nc.dram_tensor("out", (1, r_x.shape[0]), F32, kind="ExternalOutput").ap()
    bass_three_layer_mlp(nc, *args, out)
    r = run(nc, [arrays], core_ids=[0])
    return r.results[0]["out"].reshape(-1, 1)
```

```python
from contextlib import ExitStack

import concourse.bass as bass
from concourse import mybir

P = 128
NB = 512
T = 4
RING = 4

F32 = mybir.dt.float32
F32R = mybir.dt.float32r
BF16 = mybir.dt.bfloat16
U16 = mybir.dt.uint16
I32 = mybir.dt.int32
ACT = mybir.ActivationFunctionType
ALU = mybir.AluOpType
AX_X = mybir.AxisListType.X


def bass_three_layer_mlp(nc: bass.Bass, x, w1, b1, w2, b2, wout, bout, out):
    chunks = x.shape[0]
    h1_halves = w1.shape[2] // T // P
    h2_dim = w2.shape[2]
    H1 = h1_halves * P
    rounds = chunks // RING
    n_small = 5

    with ExitStack() as ctx:
        def sb(name, shape, dt=F32):
            return ctx.enter_context(nc.sbuf_tensor(name, shape, dt))

        def psum(name, shape):
            return ctx.enter_context(nc.psum_tensor(name, shape, F32))

        def sem(name):
            return ctx.enter_context(nc.semaphore(name))

        x_raw = sb("x_raw", [P, RING, T * NB])
        w_raw = sb("w_raw", [P, RING, T * H1])
        x_r = sb("x_r", [P, RING, T * NB], F32R)
        w_hi = sb("w_hi", [P, RING, T * H1], F32R)
        w_lo = sb("w_lo", [P, RING, T * H1], F32R)
        low_copy = sb("low_copy", [P, RING, T * NB], BF16)
        low_sums = sb("low_sums", [P, chunks])
        low_sum = sb("low_sum", [P, 1])
        ones = sb("ones", [P, 1])
        inexact = sb("inexact", [1, 1])
        zeros = sb("zeros", [P, NB], BF16)
        b1_sb = sb("b1_sb", [P, h1_halves])
        w2_sb = sb("w2_sb", [P, h1_halves, h2_dim])
        b2_sb = sb("b2_sb", [h2_dim, 1])
        wout_sb = sb("wout_sb", [h2_dim, 1])
        bout_sb = sb("bout_sb", [1, 1])
        h1 = sb("h1", [P, h1_halves, NB])
        h2 = sb("h2", [h2_dim, NB])
        y = sb("y", [1, NB])

        h1_ps = psum("h1_ps", [P, h1_halves, NB])
        h2_ps = psum("h2_ps", [h2_dim, NB])
        y_ps = psum("y_ps", [1, NB])
        inexact_ps = psum("inexact_ps", [1, 1])

        x_landed = [sem(f"x_landed{s}") for s in range(RING)]
        w_landed = [sem(f"w_landed{s}") for s in range(RING)]
        small_landed = sem("small_landed")
        zeros_set = sem("zeros_set")
        ones_set = sem("ones_set")
        x_rounded = sem("x_rounded")
        x_checked = sem("x_checked")
        w_hi_ready = sem("w_hi_ready")
        w_lo_ready = sem("w_lo_ready")
        slots_free = sem("slots_free")
        half_summed = [sem("half_summed0"), slots_free]
        h1_ready = [sem(f"h1_ready{m}") for m in range(h1_halves)]
        h2_summed = sem("h2_summed")
        h2_ready = sem("h2_ready")
        y_summed = sem("y_summed")
        y_ready = sem("y_ready")
        low_summed = sem("low_summed")
        inexact_summed = sem("inexact_summed")
        inexact_ready = sem("inexact_ready")
        out_stored = sem("out_stored")
        gx_landed = [sem(f"gx_landed{s}") for s in range(RING)]
        gw_landed = [sem(f"gw_landed{s}") for s in range(RING)]
        g_used = sem("g_used")

        block = ctx.enter_context(nc.Block())

        def inexact_flag(eng):
            eng.wait_ge(inexact_ready, 1)
            return eng.value_load(inexact[0:1, 0:1].bitcast(I32))

        @block.sync
        def _(sp):
            def load(c, s, x_sems, w_sems):
                sp.dma_start(w_raw[:, s, :], w1[c]).then_inc(w_sems[s], 16)
                sp.dma_start(x_raw[:, s, :], x[c]).then_inc(x_sems[s], 16)

            def store_y(n):
                sp.wait_ge(y_ready, n)
                sp.dma_start(out, y[:]).then_inc(out_stored, 16)
                sp.wait_ge(out_stored, 16 * n)

            for s in range(RING):
                load(s, s, x_landed, w_landed)
            for dst, src in ((b1_sb, b1), (w2_sb, w2), (b2_sb, b2), (wout_sb, wout), (bout_sb, bout)):
                sp.dma_start(dst[:], src).then_inc(small_landed, 16)
            with sp.Fori(0, rounds - 1) as r:
                for s in range(RING):
                    done = r * RING + (s + 1)
                    sp.wait_ge(w_lo_ready, done)
                    sp.wait_ge(x_rounded, done)
                    sp.wait_ge(x_checked, done)
                    load(r * RING + (s + RING), s, x_landed, w_landed)
            store_y(1)

            with sp.If(inexact_flag(sp) != 0):
                for s in range(RING):
                    load(s, s, gx_landed, gw_landed)
                with sp.Fori(0, rounds - 1) as r:
                    for s in range(RING):
                        sp.wait_ge(g_used, r * RING + (s + 1))
                        load(r * RING + (s + RING), s, gx_landed, gw_landed)
                store_y(2)

        @block.tensor
        def _(pe):
            def open_sums():
                for m in range(h1_halves):
                    last = nc.tensor.matmul(h1_ps[:, m, :], zeros[:, 0:P], zeros[:], start=True, stop=False,
                                            skip_group_check=True)
                return last

            def later_layers(n):
                for m in range(h1_halves):
                    pe.wait_ge(h1_ready[m], n)
                    last = nc.tensor.matmul(h2_ps[:], w2_sb[:, m, :], h1[:, m, :],
                                            start=(m == 0), stop=(m == h1_halves - 1))
                last.then_inc(h2_summed, 1)
                pe.wait_ge(h2_ready, n)
                nc.tensor.matmul(y_ps[:], wout_sb[:], h2[:], start=True, stop=True).then_inc(y_summed, 1)

            pe.wait_ge(zeros_set, 1)
            open_sums().then_inc(slots_free, RING)
            with pe.Fori(0, rounds) as r:
                for s in range(RING):
                    c = r * RING + (s + 1)
                    pe.wait_ge(w_lo_ready, c)
                    pe.wait_ge(x_rounded, c)
                    for m in range(h1_halves):
                        for t in range(T):
                            for w in (w_hi, w_lo):
                                last = nc.tensor.matmul(
                                    h1_ps[:, m, :], w[:, s, t * H1 + m * P:t * H1 + (m + 1) * P],
                                    x_r[:, s, t * NB:(t + 1) * NB], start=False, stop=False,
                                    skip_group_check=True)
                        last.then_inc(half_summed[m], 1)
            pe.wait_ge(small_landed, 16 * n_small)
            later_layers(1)
            pe.wait_ge(low_summed, 1)
            pe.wait_ge(ones_set, 1)
            nc.tensor.matmul(inexact_ps[:], low_sum[:], ones[:], start=True, stop=True).then_inc(inexact_summed, 1)

            with pe.If(inexact_flag(pe) != 0):
                open_sums()
                with pe.Fori(0, rounds) as r:
                    for s in range(RING):
                        pe.wait_ge(gw_landed[s], (r + 1) * 16)
                        pe.wait_ge(gx_landed[s], (r + 1) * 16)
                        for m in range(h1_halves):
                            for t in range(T):
                                last = nc.tensor.matmul(
                                    h1_ps[:, m, :], w_raw[:, s, t * H1 + m * P:t * H1 + (m + 1) * P],
                                    x_raw[:, s, t * NB:(t + 1) * NB], start=False, stop=False,
                                    skip_group_check=True)
                            last.then_inc(half_summed[m] if m < h1_halves - 1 else g_used, 1)
                later_layers(2)

        @block.vector
        def _(dve):
            nc.vector.memset(zeros[:], 0.0).then_inc(zeros_set, 1)
            nc.vector.memset(ones[:], 1.0).then_inc(ones_set, 1)
            with dve.Fori(0, rounds) as r:
                for s in range(RING):
                    c = r * RING + (s + 1)
                    dve.wait_ge(x_landed[s], (r + 1) * 16)
                    dve.wait_ge(slots_free, c)
                    nc.vector.tensor_copy(x_r[:, s, :], x_raw[:, s, :]).then_inc(x_rounded, 1)
                    dve.wait_ge(w_hi_ready, c)
                    nc.vector.tensor_tensor(w_lo[:, s, :], w_raw[:, s, :], w_hi[:, s, :].bitcast(F32),
                                            ALU.subtract).then_inc(w_lo_ready, 1)
            dve.wait_ge(x_checked, chunks)
            nc.vector.tensor_reduce(low_sum[:], low_sums[:], AX_X, ALU.add).then_inc(low_summed, 1)
            dve.wait_ge(inexact_summed, 1)
            nc.vector.tensor_copy(inexact[:], inexact_ps[:]).then_inc(inexact_ready, 1)

        @block.scalar
        def _(act):
            def biases_and_relus(n, halves_done):
                for m in range(h1_halves):
                    act.wait_ge(*halves_done[m])
                    nc.scalar.activation(h1[:, m, :], h1_ps[:, m, :], ACT.Relu,
                                         bias=b1_sb[:, m:m + 1]).then_inc(h1_ready[m], 1)
                act.wait_ge(h2_summed, n)
                nc.scalar.activation(h2[:], h2_ps[:], ACT.Relu, bias=b2_sb[:]).then_inc(h2_ready, 1)
                act.wait_ge(y_summed, n)
                if n > 1:
                    act.wait_ge(out_stored, 16 * (n - 1))
                nc.scalar.activation(y[:], y_ps[:], ACT.Identity, bias=bout_sb[:]).then_inc(y_ready, 1)

            with act.Fori(0, rounds) as r:
                for s in range(RING):
                    c = r * RING + (s + 1)
                    act.wait_ge(w_landed[s], (r + 1) * 16)
                    act.wait_ge(slots_free, c)
                    nc.scalar.activation(w_hi[:, s, :], w_raw[:, s, :], ACT.Copy).then_inc(w_hi_ready, 1)
                    act.wait_ge(x_landed[s], (r + 1) * 16)
                    low = x_raw[:, s, :].bitcast(U16).rearrange("p (n h) -> p n h", h=2)[:, :, 0]
                    nc.scalar.activation(low_copy[:, s, :], low, ACT.Copy,
                                         accum_out=low_sums[:, bass.ds(r * RING + s, 1)]).then_inc(x_checked, 1)
            act.wait_ge(small_landed, 16 * n_small)
            biases_and_relus(1, [(half_summed[0], chunks), (half_summed[1], RING + chunks)])
            with act.If(inexact_flag(act) != 0):
                biases_and_relus(2, [(half_summed[0], 2 * chunks), (g_used, chunks)])


def kernel(r_x, L0_rec_W1, L0_rec_b1, L0_rec_W2, L0_rec_b2, L0_rec_Wout, L0_rec_bout):
    import numpy as np
    import concourse.bacc as bacc
    from concourse.bass_utils import run_bass_kernel_spmd as run

    def chunked(a):
        rows, K = a.shape
        return np.ascontiguousarray(a.reshape(rows, K // (P * T), P, T).transpose(1, 2, 3, 0)).reshape(
            K // (P * T), P, T * rows)

    def halves(a):
        rows, H1 = a.shape
        return np.ascontiguousarray(a.reshape(rows, H1 // P, P).transpose(2, 1, 0))

    r_x, W1, b1, W2, b2, Wout, bout = (
        np.asarray(a) for a in (r_x, L0_rec_W1, L0_rec_b1, L0_rec_W2, L0_rec_b2, L0_rec_Wout, L0_rec_bout))
    arrays = {
        "x": chunked(r_x),
        "w1": chunked(W1),
        "b1": np.ascontiguousarray(b1.reshape(-1, P).T),
        "w2": halves(W2),
        "b2": b2.reshape(-1, 1),
        "wout": np.ascontiguousarray(Wout.T),
        "bout": bout.reshape(1, 1),
    }
    nc = bacc.Bacc("TRN2", target_bir_lowering=False, num_devices=1)
    args = [nc.dram_tensor(n, a.shape, mybir.dt.from_np(a.dtype), kind="ExternalInput").ap() for n, a in arrays.items()]
    out = nc.dram_tensor("out", (1, r_x.shape[0]), F32, kind="ExternalOutput").ap()
    bass_three_layer_mlp(nc, *args, out)
    r = run(nc, [arrays], core_ids=[0])
    return r.results[0]["out"].reshape(-1, 1)
```

```python
from contextlib import ExitStack

import concourse.bass as bass
from concourse import mybir

P = 128
NB = 512
T = 4
RING = 4

F32 = mybir.dt.float32
F32R = mybir.dt.float32r
BF16 = mybir.dt.bfloat16
U16 = mybir.dt.uint16
I32 = mybir.dt.int32
ACT = mybir.ActivationFunctionType
ALU = mybir.AluOpType
AX_X = mybir.AxisListType.X


def bass_three_layer_mlp(nc: bass.Bass, x, w1, b1, w2, b2, wout, bout, out):
    chunks = x.shape[0]
    halves = w1.shape[2] // T // P
    H1 = halves * P
    H2 = w2.shape[2]
    HE = H2 + 1
    blocks = NB // P
    PARTS = 2
    PART = NB // PARTS
    rounds = chunks // RING
    tiles = chunks * T
    n_small = 5

    FIRST, LAST = (0, 0), (rounds - 1, RING - 1)
    FIRST_ROUND = [(0, s) for s in range(RING)]
    CUT = {FIRST: [1, 1, 2], (rounds - 1, RING - 3): [2, 2], (rounds - 1, RING - 2): [2, 1, 1], LAST: [1] * T}

    def is_chunk(r, s, *places):
        return isinstance(r, int) and (r, s) in places

    def parts_of(r, s):
        sizes = CUT[r, s] if is_chunk(r, s, *CUT) else [T]
        return [(sum(sizes[:i]), n) for i, n in enumerate(sizes)]

    def tiles_before(r, s):
        return r * (RING * T) + s * T

    def over_chunks(eng, step):
        for s in range(RING):
            step(0, s)
        with eng.Fori(1, rounds - 1) as r:
            for s in range(RING):
                step(r, s)
        for s in range(RING):
            step(rounds - 1, s)

    def checks_before(r, s):
        if is_chunk(r, s, FIRST):
            return 0
        extra = sum(len(parts) - 1 for c, parts in CUT.items() if c == FIRST or (isinstance(r, int) and c < (r, s)))
        return r * RING + (s + extra)

    checks = checks_before(rounds, 0)

    with ExitStack() as ctx:
        def sb(name, shape, dt=F32):
            return ctx.enter_context(nc.sbuf_tensor(name, shape, dt))

        def psum(name, shape):
            return ctx.enter_context(nc.psum_tensor(name, shape, F32))

        def sem(name):
            return ctx.enter_context(nc.semaphore(name))

        x_raw = sb("x_raw", [P, RING, T * NB])
        w_raw = sb("w_raw", [P, RING, T * H1])
        x_r = sb("x_r", [P, RING, T * NB], F32R)
        w_hi = sb("w_hi", [P, RING, T * H1], F32R)
        w_lo = sb("w_lo", [P, RING, T * H1], F32R)
        low_copy = sb("low_copy", [P, RING, T * NB], BF16)
        low_sums = sb("low_sums", [P, checks])
        low_sum = sb("low_sum", [P, 1])
        inexact = sb("inexact", [1, 1])
        zeros = sb("zeros", [P, NB], BF16)
        ones = sb("ones", [P, P])
        table_warm = sb("table_warm", [P, 1])
        b1_sb = sb("b1_sb", [P, halves])
        w2_sb = sb("w2_sb", [P, halves, HE])
        b2_sb = sb("b2_sb", [1, blocks, HE])
        wout_sb = sb("wout_sb", [P, blocks, HE])
        h1 = sb("h1", [P, halves, NB])
        products = sb("products", [P, blocks, HE])
        y = sb("y", [P, blocks])

        h1_ps = psum("h1_ps", [P, halves, NB])
        h2_ps = psum("h2_ps", [P, blocks, HE])
        inexact_ps = psum("inexact_ps", [1, 1])

        x_landed = [sem(f"x_landed{s}") for s in range(RING)]
        w_landed = [sem(f"w_landed{s}") for s in range(RING)]
        early_parts = [(c, i) for c, p in CUT.items() for i in range(len(p) - 1)]
        x_part_landed = {(c, i): sem(f"x_part_landed{c[0]}_{c[1]}_{i}") for c, i in early_parts}
        w_part_landed = {(c, i): sem(f"w_part_landed{c[0]}_{c[1]}_{i}") for c, i in early_parts}
        small_landed = sem("small_landed")
        zeros_set = sem("zeros_set")
        ones_set = sem("ones_set")
        frames_set = sem("frames_set")
        x_rounded = sem("x_rounded")
        w_hi_ready = sem("w_hi_ready")
        w_lo_ready = sem("w_lo_ready")
        x_checked = sem("x_checked")
        tiles_summed = [sem(f"tiles_summed{m}") for m in range(halves)]
        h1_upper_ready = sem("h1_upper_ready")
        h1_last_ready = sem("h1_last_ready")
        h2_summed = sem("h2_summed")
        products_ready = sem("products_ready")
        y_ready = sem("y_ready")
        out_stored = sem("out_stored")
        low_summed = sem("low_summed")
        inexact_summed = sem("inexact_summed")
        inexact_ready = sem("inexact_ready")
        wout_spread = sem("wout_spread")
        gx_landed = [sem(f"gx_landed{s}") for s in range(RING)]
        gw_landed = [sem(f"gw_landed{s}") for s in range(RING)]
        g_tiles_summed = [sem(f"g_tiles_summed{m}") for m in range(halves)]

        block = ctx.enter_context(nc.Block())

        def landing(of_slot, of_part, r, s, i):
            if i == len(parts_of(r, s)) - 1:
                return of_slot[s], (r + 1) * 16
            return of_part[(r, s), i], 16

        def x_landing(r, s, i):
            return landing(x_landed, x_part_landed, r, s, i)

        def w_landing(r, s, i):
            return landing(w_landed, w_part_landed, r, s, i)

        def x_cols(t, n):
            return slice(t * NB, (t + n) * NB)

        def w_cols(t, n):
            return slice(t * H1, (t + n) * H1)

        def inexact_flag(eng):
            eng.wait_ge(inexact_ready, 1)
            return eng.value_load(inexact[0:1, 0:1].bitcast(I32))

        def half(tensor, s, t, m):
            return tensor[:, s, t * H1 + m * P:t * H1 + (m + 1) * P]

        @block.sync
        def _(sp):
            def load(r, s):
                if not is_chunk(r, s, *FIRST_ROUND):
                    sp.wait_ge(w_lo_ready, tiles_before(r - 1, s + 1))
                    sp.wait_ge(x_rounded, tiles_before(r - 1, s + 1))
                    sp.wait_ge(x_checked, tiles_before(r - 1, s + 1))
                c = r * RING + s
                for i, (t, n) in enumerate(parts_of(r, s)):
                    sp.dma_start(w_raw[:, s, w_cols(t, n)], w1[c][:, w_cols(t, n)]).then_inc(w_landing(r, s, i)[0], 16)
                    sp.dma_start(x_raw[:, s, x_cols(t, n)], x[c][:, x_cols(t, n)]).then_inc(x_landing(r, s, i)[0], 16)
                if is_chunk(r, s, (0, RING - 1)):
                    load_small()

            def load_small():
                sp.wait_ge(frames_set, 3)
                sp.dma_start(b1_sb[:], b1).then_inc(small_landed, 16)
                sp.dma_start(w2_sb[:, :, 0:H2], w2).then_inc(small_landed, 16)
                sp.dma_start(b2_sb[:, :, 0:H2], b2.unsqueeze(1).broadcast_to([1, blocks, H2])).then_inc(small_landed, 16)
                sp.dma_start(wout_sb[:, 0, 0:H2], wout.broadcast_to([P, H2])).then_inc(small_landed, 16)
                sp.dma_start(wout_sb[:, 0, H2:HE], bout.broadcast_to([P, 1])).then_inc(small_landed, 16)

            def store_y(n):
                sp.wait_ge(y_ready, n)
                sp.dma_start(out, y[:]).then_inc(out_stored, 16)
                sp.wait_ge(out_stored, 16 * n)

            over_chunks(sp, load)
            store_y(1)

            with sp.If(inexact_flag(sp) != 0):
                for s in range(RING):
                    sp.dma_start(w_raw[:, s, :], w1[s]).then_inc(gw_landed[s], 16)
                    sp.dma_start(x_raw[:, s, :], x[s]).then_inc(gx_landed[s], 16)
                with sp.Fori(1, rounds) as r:
                    for s in range(RING):
                        sp.wait_ge(g_tiles_summed[halves - 1], tiles_before(r - 1, s + 1))
                        sp.dma_start(w_raw[:, s, :], w1[r * RING + s]).then_inc(gw_landed[s], 16)
                        sp.dma_start(x_raw[:, s, :], x[r * RING + s]).then_inc(gx_landed[s], 16)
                store_y(2)

        @block.tensor
        def _(pe):
            def open_sums():
                for m in range(halves):
                    nc.tensor.matmul(h1_ps[:, m, :], zeros[:, 0:P], zeros[:], start=True, stop=False,
                                     skip_group_check=True)

            def multiply(r, s):
                if is_chunk(r, s, (rounds - 1, 0)):
                    pe.wait_ge(small_landed, 16 * n_small)
                    pe.wait_ge(ones_set, 1)
                    open_h2()
                before = tiles_before(r, s)
                parts = parts_of(r, s)
                groups = [parts[:-2], parts[-2:]] if is_chunk(r, s, LAST) else [[p] for p in parts]
                for group in groups:
                    for m in range(halves):
                        for t0, n in group:
                            if m == 0:
                                pe.wait_ge(w_lo_ready, before + (t0 + n))
                                pe.wait_ge(x_rounded, before + (t0 + n))
                            for t in range(t0, t0 + n):
                                for w in (w_lo, w_hi):
                                    last = nc.tensor.matmul(h1_ps[:, m, :], half(w, s, t, m),
                                                            x_r[:, s, t * NB:(t + 1) * NB], start=False, stop=False,
                                                            skip_group_check=True)
                        last.then_inc(tiles_summed[m], sum(n for _, n in group))

            def open_h2():
                nc.tensor.matmul(h2_ps[:], ones[0:1, :], b2_sb[:], start=True, stop=False, skip_group_check=True)

            def second_layer(n):
                for m in range(halves):
                    for j in range(blocks):
                        if m < halves - 1 and j == 0:
                            pe.wait_ge(h1_upper_ready, (halves - 1) * (n - 1) + m + 1)
                        if m == halves - 1 and j * P % PART == 0:
                            pe.wait_ge(h1_last_ready, PARTS * (n - 1) + j * P // PART + 1)
                        last = nc.tensor.matmul(h2_ps[:, j, :], h1[:, m, j * P:(j + 1) * P], w2_sb[:, m, :],
                                                start=False, stop=(m == halves - 1), skip_group_check=True)
                last.then_inc(h2_summed, 1)

            pe.wait_ge(zeros_set, 1)
            open_sums()
            over_chunks(pe, multiply)
            second_layer(1)
            pe.wait_ge(low_summed, 1)
            nc.tensor.matmul(inexact_ps[:], low_sum[:], ones[:, 0:1], start=True, stop=True).then_inc(inexact_summed, 1)

            with pe.If(inexact_flag(pe) != 0):
                open_sums()
                with pe.Fori(0, rounds) as r:
                    for s in range(RING):
                        pe.wait_ge(gw_landed[s], (r + 1) * 16)
                        pe.wait_ge(gx_landed[s], (r + 1) * 16)
                        for m in range(halves):
                            for t in range(T):
                                last = nc.tensor.matmul(h1_ps[:, m, :], half(w_raw, s, t, m),
                                                        x_raw[:, s, t * NB:(t + 1) * NB], start=False, stop=False,
                                                        skip_group_check=True)
                            last.then_inc(g_tiles_summed[m], T)
                pe.wait_ge(products_ready, 1)
                open_h2()
                second_layer(2)

        @block.vector
        def _(dve):
            nc.vector.memset(zeros[:], 0.0).then_inc(zeros_set, 1)
            nc.vector.memset(ones[:], 1.0).then_inc(ones_set, 1)
            nc.vector.memset(w2_sb[:], 0.0).then_inc(frames_set, 1)
            nc.vector.memset(b2_sb[:], 1.0).then_inc(frames_set, 1)
            nc.vector.memset(wout_sb[:], 0.0).then_inc(frames_set, 1)

            def split_w_and_round_x(r, s):
                before = tiles_before(r, s)
                if not is_chunk(r, s, *FIRST_ROUND):
                    dve.wait_ge(tiles_summed[halves - 1], tiles_before(r - 1, s + 1))
                for i, (t, n) in enumerate(parts_of(r, s)):
                    dve.wait_ge(w_hi_ready, before + (t + n))
                    w = w_cols(t, n)
                    nc.vector.tensor_tensor(w_lo[:, s, w], w_raw[:, s, w], w_hi[:, s, w].bitcast(F32),
                                            ALU.subtract).then_inc(w_lo_ready, n)
                    dve.wait_ge(*x_landing(r, s, i))
                    nc.vector.tensor_copy(x_r[:, s, x_cols(t, n)], x_raw[:, s, x_cols(t, n)]).then_inc(x_rounded, n)

            def last_half_and_last_layer(n, summed):
                m = halves - 1
                dve.wait_ge(summed[m], tiles)
                for j in range(PARTS):
                    rows = slice(j * PART, (j + 1) * PART)
                    nc.vector.tensor_scalar(h1[:, m, rows], h1_ps[:, m, rows], b1_sb[:, m:m + 1], 0.0,
                                            ALU.add, ALU.max).then_inc(h1_last_ready, 1)
                dve.wait_ge(h2_summed, n)
                nc.vector.scalar_tensor_tensor(products[:], h2_ps[:], 0.0, wout_sb[:], ALU.max,
                                               ALU.mult).then_inc(products_ready, 1)
                dve.wait_ge(products_ready, n)
                if n > 1:
                    dve.wait_ge(out_stored, 16 * (n - 1))
                nc.vector.tensor_reduce(y[:], products[:], AX_X, ALU.add).then_inc(y_ready, 1)

            def spread_wout():
                for j in range(1, blocks):
                    last = nc.vector.tensor_copy(wout_sb[:, j, :], wout_sb[:, 0, :])
                last.then_inc(wout_spread, 1)

            over_chunks(dve, split_w_and_round_x)
            dve.wait_ge(small_landed, 16 * n_small)
            spread_wout()
            dve.wait_ge(wout_spread, 1)
            last_half_and_last_layer(1, tiles_summed)
            dve.wait_ge(x_checked, tiles)
            nc.vector.tensor_reduce(low_sum[:], low_sums[:], AX_X, ALU.add).then_inc(low_summed, 1)
            dve.wait_ge(inexact_summed, 1)
            nc.vector.tensor_copy(inexact[:], inexact_ps[:]).then_inc(inexact_ready, 1)

            with dve.If(inexact_flag(dve) != 0):
                last_half_and_last_layer(2, g_tiles_summed)

        @block.scalar
        def _(act):
            act.wait_ge(zeros_set, 1)
            nc.scalar.activation(table_warm[:], zeros[:, 0:1], ACT.Relu)

            def top_of_w_and_check_x(r, s):
                if not is_chunk(r, s, *FIRST_ROUND):
                    act.wait_ge(tiles_summed[halves - 1], tiles_before(r - 1, s + 1))
                parts = parts_of(r, s)

                def top_of_w(i, t, n):
                    act.wait_ge(*w_landing(r, s, i))
                    nc.scalar.activation(w_hi[:, s, w_cols(t, n)], w_raw[:, s, w_cols(t, n)],
                                         ACT.Copy).then_inc(w_hi_ready, n)

                def check_x(i, t, n):
                    act.wait_ge(*x_landing(r, s, i))
                    low = x_raw[:, s, x_cols(t, n)].bitcast(U16).rearrange("p (n h) -> p n h", h=2)[:, :, 0]
                    nc.scalar.activation(low_copy[:, s, x_cols(t, n)], low, ACT.Copy,
                                         accum_out=low_sums[:, bass.ds(checks_before(r, s) + i, 1)]).then_inc(x_checked, n)

                top_of_w(0, *parts[0])
                for i in range(len(parts)):
                    if i + 1 < len(parts):
                        top_of_w(i + 1, *parts[i + 1])
                    check_x(i, *parts[i])

            def upper_half(summed):
                for m in range(halves - 1):
                    act.wait_ge(summed[m], tiles)
                    nc.scalar.activation(h1[:, m, :], h1_ps[:, m, :], ACT.Relu,
                                         bias=b1_sb[:, m:m + 1]).then_inc(h1_upper_ready, 1)

            over_chunks(act, top_of_w_and_check_x)
            act.wait_ge(small_landed, 16 * n_small)
            upper_half(tiles_summed)

            with act.If(inexact_flag(act) != 0):
                upper_half(g_tiles_summed)


def kernel(r_x, L0_rec_W1, L0_rec_b1, L0_rec_W2, L0_rec_b2, L0_rec_Wout, L0_rec_bout):
    import numpy as np
    import concourse.bacc as bacc
    from concourse.bass_utils import run_bass_kernel_spmd as run

    def chunked(a):
        rows, K = a.shape
        return np.ascontiguousarray(a.reshape(rows, K // (P * T), P, T).transpose(1, 2, 3, 0)).reshape(
            K // (P * T), P, T * rows)

    def halves(a):
        rows, H1 = a.shape
        return np.ascontiguousarray(a.reshape(rows, H1 // P, P).transpose(2, 1, 0))

    r_x, W1, b1, W2, b2, Wout, bout = (
        np.asarray(a) for a in (r_x, L0_rec_W1, L0_rec_b1, L0_rec_W2, L0_rec_b2, L0_rec_Wout, L0_rec_bout))
    arrays = {
        "x": chunked(r_x),
        "w1": chunked(W1),
        "b1": np.ascontiguousarray(b1.reshape(-1, P).T),
        "w2": halves(W2),
        "b2": b2.reshape(1, -1),
        "wout": Wout,
        "bout": bout.reshape(1, 1),
    }
    nc = bacc.Bacc("TRN2", target_bir_lowering=False, num_devices=1)
    args = [nc.dram_tensor(n, a.shape, mybir.dt.from_np(a.dtype), kind="ExternalInput").ap() for n, a in arrays.items()]
    out = nc.dram_tensor("out", (P, r_x.shape[0] // P), F32, kind="ExternalOutput").ap()
    bass_three_layer_mlp(nc, *args, out)
    r = run(nc, [arrays], core_ids=[0])
    return np.ascontiguousarray(r.results[0]["out"].T).reshape(-1, 1)
```
